# Optimizing a Trainium2 kernel written in Bass

```python
import numpy as np
import jax
import jax.numpy as jnp

def _softmax(x, axis=-1):
    return jax.nn.softmax(x, axis=axis)

def _gelu(x):
    return jax.nn.gelu(x, approximate=True)

def _silu(x):
    return jax.nn.silu(x)

def _sigmoid(x):
    return jax.nn.sigmoid(x)

def _layernorm(x, axis=-1, eps=1e-05):
    m = jnp.mean(x, axis=axis, keepdims=True)
    v = jnp.var(x, axis=axis, keepdims=True)
    return (x - m) / jnp.sqrt(v + eps)

def _scatter_add(tgt, idx, src, axis=0):
    return tgt.at[idx].add(src)

def _segment_sum(src, seg, n):
    return jax.ops.segment_sum(src, seg, n)
kernel_name = 'mk_adj_preln_d1_adj_r2_330335'

def setup_inputs(seed: int=0):
    np.random.seed(seed)
    _w = jnp.asarray

    def _rec_inputs():
        import jax
        import jax.numpy as jnp
        _gk = jax.random.key(seed)
        x = -0.003407 + 1.001 * jax.random.normal(jax.random.fold_in(_gk, 1), (64, 128, 128), jnp.float32)
        _a = jax.random.bernoulli(jax.random.fold_in(_gk, 2), 0.015625, (64, 128, 128))
        _a = jnp.logical_or(_a, jnp.swapaxes(_a, -1, -2))
        _a = jnp.logical_or(_a, jnp.eye(128, dtype=bool))
        _af = _a.astype(jnp.float32)
        _af = _af * jax.random.uniform(jax.random.fold_in(_gk, 3), (64, 128, 128), jnp.float32, 0.05, 1)
        adj = _af
        return (x, adj)
    x, adj = _rec_inputs()

    def _L0_gnn_setup():
        import jax, jax.numpy as jnp
        import numpy as np
        B, S, H, HID = (1, 512, 128, 128)
        LN_EPS = 1e-05

        def _layernorm(y, gamma, beta):
            mu = jnp.mean(y, axis=-1, keepdims=True)
            var = jnp.mean(jnp.square(y - mu), axis=-1, keepdims=True)
            return (y - mu) * jax.lax.rsqrt(var + LN_EPS) * gamma + beta
        key = jax.random.key(seed)
        ks = jax.random.split(key, 8)
        x = jax.random.normal(ks[0], (B, S, H), dtype=jnp.float32)
        adj = jax.random.uniform(ks[1], (B, S, S), dtype=jnp.float32)
        W1 = jax.random.normal(ks[2], (2 * H, HID), dtype=jnp.float32) / np.sqrt(2 * H)
        b1 = jnp.zeros((HID,), dtype=jnp.float32)
        W2 = jax.random.normal(ks[3], (HID, HID), dtype=jnp.float32) / np.sqrt(HID)
        b2 = jnp.zeros((HID,), dtype=jnp.float32)
        gamma = jnp.ones((HID,), dtype=jnp.float32)
        beta = jnp.zeros((HID,), dtype=jnp.float32)
        return {'x': x, 'adj': adj, 'W1': W1, 'b1': b1, 'W2': W2, 'b2': b2, 'gamma': gamma, 'beta': beta}
    _L0_gnn_all = _L0_gnn_setup()
    _L0_gnn_in = {k: v for k, v in _L0_gnn_all.items() if k in ('W1', 'b1', 'W2', 'b2', 'gamma', 'beta')}
    del _L0_gnn_all
    return {'x': x, 'adj': adj, 'L0_gnn_W1': _L0_gnn_in['W1'], 'L0_gnn_b1': _L0_gnn_in['b1'], 'L0_gnn_W2': _L0_gnn_in['W2'], 'L0_gnn_b2': _L0_gnn_in['b2'], 'L0_gnn_gamma': _L0_gnn_in['gamma'], 'L0_gnn_beta': _L0_gnn_in['beta']}

def reference(x, adj, L0_gnn_W1, L0_gnn_b1, L0_gnn_W2, L0_gnn_b2, L0_gnn_gamma, L0_gnn_beta):
    import jax
    import jax.numpy as jnp

    def _L0_gnn_ref(x, adj, W1, b1, W2, b2, gamma, beta):
        import jax, jax.numpy as jnp
        import numpy as np
        B, S, H, HID = (1, 512, 128, 128)
        LN_EPS = 1e-05

        def _layernorm(y, gamma, beta):
            mu = jnp.mean(y, axis=-1, keepdims=True)
            var = jnp.mean(jnp.square(y - mu), axis=-1, keepdims=True)
            return (y - mu) * jax.lax.rsqrt(var + LN_EPS) * gamma + beta
        hi = jnp.einsum('bsh,hk->bsk', x, W1[:H])
        hj = jnp.einsum('bsh,hk->bsk', x, W1[H:])
        h = jax.nn.relu(hi[:, :, None, :] + hj[:, None, :, :] + b1)
        y = jnp.einsum('bijk,kl->bijl', h, W2) + b2
        y = _layernorm(y, gamma, beta)
        out = jnp.einsum('bij,bijh->bih', adj, y)
        return out
    h = jnp.maximum(_layernorm(x, axis=-1), 0.0)
    x = x + _L0_gnn_ref(h, adj, L0_gnn_W1, L0_gnn_b1, L0_gnn_W2, L0_gnn_b2, L0_gnn_gamma, L0_gnn_beta)
    return x

_drawn_inputs = setup_inputs


def setup_inputs(seed=0):
    import zlib

    import numpy as np

    out = dict(_drawn_inputs(seed))
    spreads = {'L0_gnn_b1': (0.0, 0.1),
     'L0_gnn_b2': (0.0, 0.1),
     'L0_gnn_gamma': (1.0, 0.2),
     'L0_gnn_beta': (0.0, 0.1)}
    factors = {}
    for name, (base, spread) in spreads.items():
        noise = np.random.default_rng([zlib.crc32(name.encode()), seed]).standard_normal(out[name].shape)
        drawn = base * np.exp(spread * noise) if base else spread * noise
        out[name] = jnp.asarray(drawn.astype(out[name].dtype))
    for name, factor in factors.items():
        out[name] = (out[name] * factor).astype(out[name].dtype)
    return out
```

```python
import concourse.bass as bass
from concourse import mybir
from contextlib import ExitStack


def gnn_layer(nc, x, adj, w1, b1, w2, b2, gamma, beta, out):
    F32, F32R, F16, BF16, I32 = (mybir.dt.float32, mybir.dt.float32r, mybir.dt.float16,
                                 mybir.dt.bfloat16, mybir.dt.int32)
    ALU, ACT, AX = mybir.AluOpType, mybir.ActivationFunctionType, mybir.AxisListType

    BATCHES, NODES, FEAT = x.shape
    P = 128
    CHUNKS = 6
    EDGES = CHUNKS * P
    HALF = EDGES // 2
    WINDOWS = -(-NODES * NODES // EDGES)
    GB = 4
    GROUPS = BATCHES // GB
    BODY = 2 * GB
    HEAD = 2 * GB
    LOOPED = BATCHES - HEAD - BODY
    EPS = 1e-05
    assert NODES == P and FEAT == P and LOOPED % BODY == 0

    x_d = x.rearrange("b n f -> n b f")
    adj_d = adj.rearrange("b n m -> n b m")
    out_d = out.rearrange("b n f -> n b f")

    ctx = ExitStack()
    with ctx:
        def sb(name, shape, dt=F32):
            return ctx.enter_context(nc.sbuf_tensor(name, shape, dt))

        def pb(name, shape, dt=F32):
            return ctx.enter_context(nc.psum_tensor(name, shape, dt))

        def sem(name):
            return ctx.enter_context(nc.semaphore(name))

        ident = sb("ident", [P, P])
        before = sb("before", [P, P], BF16)
        upto = sb("upto", [P, P], BF16)
        minus_half = sb("minus_half", [P, CHUNKS])
        eps_x = sb("eps_x", [P, GB])
        eps_z = sb("eps_z", [P, CHUNKS])
        tri = sb("tri", [P, P])
        ones = sb("ones", [P, P], BF16)
        ones_f = sb("ones_f", [P, P])
        position_f = sb("position_f", [P, EDGES])
        position = sb("position", [P, EDGES], F16)
        number = sb("number", [P, EDGES], F16)
        number_col = sb("number_col", [P, CHUNKS])
        restart = sb("restart", [P, GB * P], BF16)
        w1_sb = sb("w1_sb", [P, 2 * P])
        b1_col = sb("b1_col", [P, 1])
        w2_in = sb("w2_in", [P, P])
        w2_c = sb("w2_c", [P, P])
        b2_all = sb("b2_all", [P, P])
        b2_c = sb("b2_c", [P, P])
        b2_part = sb("b2_part", [P, 3, P], BF16)
        b2_rest = sb("b2_rest", [P, 2, P])
        b2_rows = sb("b2_rows", [P, 3, P], BF16)
        b2_k = sb("b2_k", [P, P], BF16)
        mean_w = sb("mean_w", [P, 2])
        gamma_all = sb("gamma_all", [P, P])
        gamma_s = sb("gamma_s", [P, P])
        beta_all = sb("beta_all", [P, P])
        window = sb("window", [P, 1])
        most = sb("most", [P, GB])
        most_1 = sb("most_1", [P, 1])
        most_i = sb("most_i", [P, 1], I32)

        x_g = [sb(f"x_g{i}", [P, GB, P]) for i in range(2)]
        adj_g = [sb(f"adj_g{i}", [P, GB, P]) for i in range(2)]
        res_g = [sb(f"res_g{i}", [P, GB, P]) for i in range(2)]
        out_g = [sb(f"out_g{i}", [P, GB, P]) for i in range(2)]
        edge_g = [sb(f"edge_g{i}", [P, GB * P], BF16) for i in range(2)]
        rank_g = [sb(f"rank_g{i}", [P, GB * P]) for i in range(2)]
        count_g = sb("count_g", [P, GB], BF16)
        bound_g = [sb(f"bound_g{i}", [P, 2 * GB]) for i in range(2)]
        stats_g = sb("stats_g", [P, GB, 6])
        mv_g = [sb(f"mv_g{i}", [P, GB, 2]) for i in range(2)]
        rstd_g = [sb(f"rstd_g{i}", [P, GB]) for i in range(2)]
        degree_g = [sb(f"degree_g{i}", [P, GB]) for i in range(2)]

        r = sb("r", [P, P])
        rT = sb("rT", [P, P])
        numbers = [sb(f"numbers{i}", [P, P], F32R) for i in range(2)]
        past = sb("past", [P, EDGES], F16)
        src_hot = [sb(f"src_hot{i}", [P, EDGES], F32R) for i in range(2)]
        dst_hot = sb("dst_hot", [P, EDGES], F32R)
        proj_hi = [sb(f"proj_hi{i}", [P, 2 * P], F32R) for i in range(2)]
        proj_lo = [sb(f"proj_lo{i}", [P, 2 * P], F32R) for i in range(2)]
        table = [sb(f"table{i}", [P, 4 * P], F32R) for i in range(2)]
        hidden = sb("hidden", [P, EDGES])
        z_sb = [sb(f"z_sb{i}", [P, EDGES]) for i in range(2)]
        square = sb("square", [P, EDGES])
        sumsq = sb("sumsq", [P, CHUNKS])
        rstd = sb("rstd", [P, CHUNKS])
        own = sb("own", [P, EDGES], BF16)
        weight = [sb(f"weight{i}", [P, EDGES]) for i in range(4)]
        scaled = [sb(f"scaled{i}", [P, P]) for i in range(2)]
        xvar = sb("xvar", [P, GB])
        var = sb("var", [P, CHUNKS])
        beta_x = sb("beta_x", [P, P])

        bankA = pb("bankA", [P, 2, 512])
        bankZ = pb("bankZ", [P, 2, 512])
        bankW = pb("bankW", [P, CHUNKS, 2 * P])
        bankH = pb("bankH", [P, 512])
        edges_ps = bankA[:, :, 0:HALF]
        z_ps = bankZ[:, :, 0:HALF]
        out_ps = bankH[:, 0:P]
        bound_ps = bankH[:, 2 * P:2 * P + 2 * GB]
        xT_ps = bankH[:, 0:P]
        proj_ps = bankH[:, 0:2 * P]
        adjT_ps = bankH[:, 2 * P:3 * P]
        numT_ps = bankH[:, 3 * P:4 * P]

        def halves(t):
            return t.rearrange("p (a n) -> p a n", a=2)

        def chunk(t, k):
            return t[:, k * P:(k + 1) * P]

        def z_chunk(k):
            return bankZ[:, k // 3, (k % 3) * P:(k % 3 + 1) * P]

        r_done = sem("r_done")
        xT_done = sem("xT_done")
        rT_done = sem("rT_done")
        hi_done = sem("hi_done")
        lo_done = sem("lo_done")
        numbers_done = sem("numbers_done")
        past_done = sem("past_done")
        src_done = sem("src_done")
        tableT_done = sem("tableT_done")
        table_done = sem("table_done")
        adj_lo_done = sem("adj_lo_done")
        found_done = sem("found_done")
        dst_done = sem("dst_done")
        pre_done = sem("pre_done")
        hidden_done = sem("hidden_done")
        z_done = sem("z_done")
        sumsq_done = sem("sumsq_done")
        z_sb_done = sem("z_sb_done")
        var_done = sem("var_done")
        rstd_done = sem("rstd_done")
        rows_done = sem("rows_done")
        own_done = sem("own_done")
        weight_done = sem("weight_done")
        sum_done = sem("sum_done")
        scaled_done = sem("scaled_done")
        beta_done = sem("beta_done")
        base_done = sem("base_done")
        out_done = sem("out_done")
        edge_done = sem("edge_done")
        rank_done = sem("rank_done")
        count_done = sem("count_done")
        boundmm_done = sem("boundmm_done")
        bound_done = sem("bound_done")
        stats_done = sem("stats_done")
        mean_done = sem("mean_done")
        xvar_done = sem("xvar_done")
        xrstd_done = sem("xrstd_done")
        degree_done = sem("degree_done")
        x_in = [sem(f"x_in{i}") for i in range(2)]
        adj_in = [sem(f"adj_in{i}") for i in range(2)]
        res_in = [sem(f"res_in{i}") for i in range(2)]
        stored = [sem(f"stored{i}") for i in range(2)]
        params_in = sem("params_in")
        pool_set = sem("pool_set")
        const_set = sem("const_set")
        window_set = sem("window_set")
        flag_step = sem("flag_step")
        flag_set = sem("flag_set")

        block = ctx.enter_context(nc.Block())

        def reach(eng, s, value):
            if not isinstance(value, int) or value > 0:
                eng.wait_ge(s, value)

        def sweep(eng, step, done):
            for c in range(-3, HEAD):
                step(0, done, c, lambda b: 0 <= b < BATCHES)
            with eng.Fori(0, LOOPED - BODY + 1, BODY) as m:
                for c in range(HEAD, HEAD + BODY):
                    step(m, m + done, c, lambda b: True)
            for c in range(HEAD + LOOPED, BATCHES + GB):
                step(0, done, c, lambda b: 0 <= b < BATCHES)

        def sweeps(eng, make):
            sweep(eng, make(True), 0)
            if make.__name__ == "vector_steps":
                make.flag()
            eng.wait_ge(flag_set, 1)
            edges = eng.value_load(most_i[P - 1:P, 0:1], min_val=0, max_val=NODES * NODES)
            with eng.If(edges > EDGES):
                with eng.Fori(BATCHES, BATCHES * WINDOWS, BATCHES) as done:
                    if make.__name__ == "vector_steps":
                        make.advance(done)
                    sweep(eng, make(False), done)

        def groups_of(v, g):
            return (v // GB if isinstance(v, int) else v * 1 // GB) + g + 1

        def loads_of(v, g):
            return v * (16 // (2 * GB)) + 16 * (g // 2 + 1)

        @block.sync
        def _(sp):
            sp.dma_start(x_g[0][:, :, :], x_d[:, 0:GB, :]).then_inc(x_in[0], 16)
            sp.dma_start(adj_g[0][:, :, :], adj_d[:, 0:GB, :]).then_inc(adj_in[0], 16)
            for dst, src in ((w1_sb[:, 0:P], w1[0:P, :]), (w1_sb[:, P:2 * P], w1[P:2 * P, :]),
                             (b1_col[:, :], b1.rearrange("(k a) -> k a", a=1)), (w2_in[:, :], w2),
                             (b2_all[:, :], b2.partition_broadcast(P)),
                             (gamma_all[:, :], gamma.partition_broadcast(P)),
                             (beta_all[:, :], beta.partition_broadcast(P))):
                sp.dma_start(dst, src).then_inc(params_in, 16)

            def held(value):
                return value if isinstance(value, int) else sp.snap(value)

            def sync_steps(first):
                def step(m, v, c, live):
                    if c % GB == 3 and live(c - 4):
                        g = (c - 4) // GB
                        at = bass.ds(held(m + GB * g), GB)
                        sp.wait_ge(out_done, v + c - 4 + 1)
                        sp.dma_start(out_d[:, at, :], out_g[g % 2][:, :, :]).then_inc(stored[g % 2], 16)
                    g = c // GB + 1
                    if (c % GB == 0 or c == -3 and not first) and live(GB * g):
                        i = g % 2
                        at = bass.ds(held(m + GB * g), GB)
                        used = held(v + GB * (g - 1))
                        if not first:
                            used_out = held(v + GB * (g - 2) + GB)
                            last_store = held(loads_of(v, g) - 16 * GROUPS // 2)
                        if first:
                            reach(sp, base_done, used)
                        reach(sp, r_done, used)
                        reach(sp, tableT_done, used)
                        sp.dma_start(x_g[i][:, :, :], x_d[:, at, :]).then_inc(x_in[i], 16)
                        sp.dma_start(adj_g[i][:, :, :], adj_d[:, at, :]).then_inc(adj_in[i], 16)
                        if not first:
                            sp.wait_ge(stored[i], last_store)
                            sp.wait_ge(out_done, used_out)
                            sp.dma_start(res_g[i][:, :, :], out_d[:, at, :]).then_inc(res_in[i], 16)
                return step

            def all_stored(windows):
                for i in range(2):
                    sp.wait_ge(stored[i], 16 * (GROUPS // 2) * windows)

            sweep(sp, sync_steps(True), 0)
            all_stored(1)
            sp.wait_ge(flag_set, 1)
            edges = sp.value_load(most_i[P - 1:P, 0:1], min_val=0, max_val=NODES * NODES)
            with sp.If(edges > EDGES):
                with sp.Fori(BATCHES, BATCHES * WINDOWS, BATCHES) as done:
                    sweep(sp, sync_steps(False), done)
                all_stored(WINDOWS)

        @block.gpsimd
        def _(pool):
            pool.iota(position_f[:, :], [[1, EDGES]], base=0, channel_multiplier=0,
                      allow_small_or_imprecise_dtypes=True).then_inc(pool_set, 1)
            pool.iota(number_col[:, :], [[P, CHUNKS]], base=1, channel_multiplier=1,
                      allow_small_or_imprecise_dtypes=True).then_inc(pool_set, 1)
            pool.memset(ones_f[:, :], 1.0).then_inc(pool_set, 1)
            pool.memset(minus_half[:, :], -0.5).then_inc(pool_set, 1)
            pool.memset(eps_x[:, :], EPS).then_inc(pool_set, 1)
            pool.memset(eps_z[:, :], EPS * FEAT).then_inc(pool_set, 1)
            pool.wait_ge(pool_set, 6)
            for dst, op, base in ((ident, ALU.is_equal, 0), (tri, ALU.is_gt, 0)):
                pool.affine_select(out=dst[:, :], in_=ones_f[:, :], compare_op=op, fill=0.0, base=base,
                                   pattern=[[1, P]], channel_multiplier=-1).then_inc(pool_set, 1)

            def pool_steps(first):
                def step(m, v, c, live):
                    b = c
                    if live(b) and first:
                        g, k = b // GB, b % GB
                        pool.wait_ge(degree_done, (m // GB) + g + 1)
                        pool.wait_ge(x_in[g % 2], loads_of(v, g))
                        reach(pool, stored[g % 2], loads_of(v, g - 2))
                        reach(pool, base_done, v + b)
                        pool.tensor_tensor(beta_x[:, :], beta_all[:, :],
                                           degree_g[g % 2][:, k:k + 1].to_broadcast([P, P]),
                                           ALU.mult).then_inc(beta_done, 1)
                        pool.wait_ge(beta_done, v + b + 1)
                        pool.tensor_tensor(out_g[g % 2][:, k, :], x_g[g % 2][:, k, :], beta_x[:, :],
                                           ALU.add).then_inc(base_done, 1)
                    if live(c - 1):
                        b = c - 1
                        pool.wait_ge(sumsq_done, v + b + 1)
                        reach(pool, z_sb_done, v + b)
                        pool.tensor_tensor(var[:, :], sumsq[:, :], eps_z[:, :],
                                           ALU.add).then_inc(var_done, 1)
                        pool.wait_ge(var_done, v + b + 1)
                        pool.tensor_tensor(rstd[:, :], var[:, :], minus_half[:, :],
                                           ALU.pow).then_inc(rstd_done, 1)
                    b = c - 3
                    if live(b):
                        g, k = b // GB, b % GB
                        if first:
                            base = out_g[g % 2]
                            pool.wait_ge(base_done, v + b + 1)
                        else:
                            base = res_g[g % 2]
                            pool.wait_ge(res_in[g % 2], loads_of(v, g) - 16 * GROUPS // 2)
                            pool.wait_ge(stored[g % 2], loads_of(v, g - 2))
                        pool.wait_ge(scaled_done, v + b + 1)
                        pool.tensor_tensor(out_g[g % 2][:, k, :], base[:, k, :], scaled[b % 2][:, :],
                                           ALU.add).then_inc(out_done, 1)
                    if c % GB == 2 and live(c + 2):
                        g = (c + 2) // GB
                        pool.wait_ge(mean_done, groups_of(v, g))
                        reach(pool, xrstd_done, groups_of(v, g - 1))
                        pool.tensor_tensor(xvar[:, :], mv_g[g % 2][:, :, 1], eps_x[:, :],
                                           ALU.add).then_inc(xvar_done, 1)
                        pool.wait_ge(xvar_done, groups_of(v, g))
                        pool.tensor_tensor(rstd_g[g % 2][:, :], xvar[:, :], minus_half[:, 0:GB],
                                           ALU.pow).then_inc(xrstd_done, 1)
                return step
            sweeps(pool, pool_steps)

        @block.scalar
        def _(act):
            act.wait_ge(const_set, 1)

            def scalar_steps(first):
                def step(m, v, c, live):
                    if live(c + 1):
                        b = c + 1
                        act.wait_ge(xT_done, v + b + 1)
                        act.activation(rT[:, :], xT_ps, ACT.Copy).then_inc(rT_done, 1)
                    if live(c - 1):
                        b = c - 1
                        act.wait_ge(z_done, v + b + 1)
                        reach(act, rstd_done, v + b)
                        for k in range(CHUNKS):
                            last = act.activation(chunk(square, k), z_chunk(k), ACT.Square,
                                                  accum_out=sumsq[:, k:k + 1])
                        last.then_inc(sumsq_done, 1)
                    if live(c + 1):
                        b = c + 1
                        g, k = b // GB, b % GB
                        act.wait_ge(tableT_done, v + b + 1)
                        act.wait_ge(xrstd_done, groups_of(v, g))
                        act.activation(proj_hi[b % 2][:, :], proj_ps, ACT.Copy,
                                       scale=rstd_g[g % 2][:, k:k + 1]).then_inc(hi_done, 1)
                        act.activation(table[b % 2][:, 0:2 * P], bankH[:, 2 * P:4 * P], ACT.Copy)\
                           .then_inc(table_done, 1)
                    if live(c):
                        b = c
                        act.wait_ge(pre_done, v + b + 1)
                        act.activation(halves(hidden[:, :]), edges_ps, ACT.Relu, bias=b1_col[:, 0:1])\
                           .then_inc(hidden_done, 1)
                    if live(c - 1):
                        b = c - 1
                        act.wait_ge(rstd_done, v + b + 1)
                        reach(act, sum_done, v + b - 1)
                        for k in range(CHUNKS):
                            last = act.activation(chunk(z_sb[b % 2], k), z_chunk(k), ACT.Copy,
                                                  scale=rstd[:, k:k + 1])
                        last.then_inc(z_sb_done, 1)
                return step
            sweeps(act, scalar_steps)

        @block.vector
        def _(dve):
            made = [0]

            def then(ins):
                made[0] += 1
                ins.then_inc(window_set, 1)
                dve.wait_ge(window_set, made[0])

            then(dve.memset(restart[:, :], 1.0))
            dve.memset(ones[:, :], 1.0)
            dve.memset(window[:, :], 0.0)
            dve.memset(most[:, :], 0.0)
            for t in table:
                dve.memset(t[:, 3 * P:4 * P].bitcast(F32), 0.0)
            then(dve.memset(restart[:, :].rearrange("p (b n) -> p b n", b=GB)[:, :, 0:1], 0.0))
            dve.wait_ge(pool_set, 8)
            dve.tensor_copy(position[:, :], position_f[:, :])
            dve.tensor_scalar(number[:, :], position_f[:, :], 1.0, None, ALU.add)
            dve.tensor_copy(before[:, :], tri[:, :])
            then(dve.tensor_tensor(upto[:, :], tri[:, :], ident[:, :], ALU.add))
            dve.wait_ge(params_in, 16 * 7)
            dve.tensor_reduce(mean_w[:, 0:1], w2_in[:, :], AX.X, ALU.add)
            then(dve.tensor_reduce(mean_w[:, 1:2], b2_all[:, :], AX.X, ALU.add))
            then(dve.tensor_scalar(mean_w[:, :], mean_w[:, :], 1.0 / FEAT, None, ALU.mult))
            dve.tensor_scalar(w2_c[:, :], w2_in[:, :], mean_w[:, 0:1], None, ALU.subtract)
            then(dve.tensor_scalar(b2_c[:, :], b2_all[:, :], mean_w[:, 1:2], None, ALU.subtract))
            then(dve.tensor_copy(b2_part[:, 0, :], b2_c[:, :]))
            then(dve.tensor_tensor(b2_rest[:, 0, :], b2_c[:, :], b2_part[:, 0, :], ALU.subtract))
            then(dve.tensor_copy(b2_part[:, 1, :], b2_rest[:, 0, :]))
            then(dve.tensor_tensor(b2_rest[:, 1, :], b2_rest[:, 0, :], b2_part[:, 1, :], ALU.subtract))
            then(dve.tensor_copy(b2_part[:, 2, :], b2_rest[:, 1, :]))
            for n in range(3):
                last = dve.tensor_scalar(b2_rows[:, n, :], b2_part[:, n, :], ident[:, n:n + 1], None, ALU.mult)
            then(last)
            then(dve.tensor_tensor(b2_rows[:, 0, :], b2_rows[:, 0, :], b2_rows[:, 1, :], ALU.add))
            dve.tensor_tensor(b2_k[:, :], b2_rows[:, 0, :], b2_rows[:, 2, :], ALU.add)
            dve.tensor_scalar(gamma_s[:, :], gamma_all[:, :], float(FEAT) ** 0.5, None, ALU.mult)\
               .then_inc(const_set, 1)

            def vector_steps(first):
                def step(m, v, c, live):
                    if live(c - 3):
                        b = c - 3
                        dve.wait_ge(sum_done, v + b + 1)
                        reach(dve, out_done, v + b - 1)
                        dve.tensor_tensor(scaled[b % 2][:, :], out_ps, gamma_s[:, :],
                                          ALU.mult).then_inc(scaled_done, 1)
                    if c % GB == 3 and live(c + 1):
                        g = (c + 1) // GB
                        i = g % 2
                        dve.wait_ge(boundmm_done, groups_of(v, g))
                        if first:
                            dve.tensor_tensor(most[:, :], bound_ps[:, GB:2 * GB], most[:, :], ALU.max)\
                               .then_inc(flag_step, 1)
                        dve.tensor_scalar(bound_g[i][:, :], bound_ps, window[:, 0:1], None, ALU.subtract)\
                           .then_inc(bound_done, 1)
                    if live(c):
                        b = c
                        dve.wait_ge(found_done, v + b + 1)
                        dve.tensor_tensor(halves(dst_hot[:, :]), edges_ps, halves(number[:, :]),
                                          ALU.is_equal).then_inc(dst_done, 1)
                    if live(c - 1):
                        b = c - 1
                        dve.wait_ge(own_done, v + b + 1)
                        reach(dve, sum_done, v + b - 3)
                        dve.tensor_tensor(weight[b % 4][:, :].rearrange("p (k n) -> p k n", k=CHUNKS),
                                          bankW[:, :, 0:P],
                                          own[:, :].rearrange("p (k n) -> p k n", k=CHUNKS),
                                          ALU.mult).then_inc(weight_done, 1)
                    if c % GB == 2 and live(c + 2):
                        g = (c + 2) // GB
                        i = g % 2
                        dve.wait_ge(x_in[i], loads_of(v, g))
                        for k in range(GB):
                            last = dve.bn_stats(stats_g[:, k, :], x_g[i][:, k, :])
                        last.then_inc(stats_done, 1)
                    if live(c + 1):
                        b = c + 1
                        g, k = b // GB, b % GB
                        at = slice(k * P, (k + 1) * P)
                        first_edge = bound_g[g % 2][:, k:k + 1]
                        end_edge = bound_g[g % 2][:, GB + k:GB + k + 1]
                        dve.wait_ge(bound_done, groups_of(v, g))
                        dve.scalar_tensor_tensor(numbers[b % 2][:, :], rank_g[g % 2][:, at], first_edge,
                                                 edge_g[g % 2][:, at], ALU.add, ALU.mult)\
                           .then_inc(numbers_done, 1)
                        dve.tensor_scalar(past[:, :], position[:, :], end_edge, None, ALU.is_ge)\
                           .then_inc(past_done, 1)
                        dve.wait_ge(past_done, v + b + 1)
                        dve.scalar_tensor_tensor(src_hot[b % 2][:, :], position[:, :], first_edge,
                                                 past[:, :], ALU.is_ge, ALU.subtract)\
                           .then_inc(src_done, 1)
                    if c % GB == 1 and live(c + 3):
                        g = (c + 3) // GB
                        i = g % 2
                        dve.wait_ge(adj_in[i], loads_of(v, g))
                        dve.tensor_scalar(edge_g[i][:, :], adj_g[i][:, :, :].rearrange("p b n -> p (b n)"),
                                          0.0, None, ALU.not_equal).then_inc(edge_done, 1)
                        dve.wait_ge(edge_done, groups_of(v, g))
                        dve.tensor_tensor_scan(rank_g[i][:, :], restart[:, :], edge_g[i][:, :], 0.0,
                                               ALU.mult, ALU.add).then_inc(rank_done, 1)
                    if c % GB == 2 and live(c + 2):
                        g = (c + 2) // GB
                        i = g % 2
                        dve.wait_ge(stats_done, groups_of(v, g))
                        dve.wait_ge(rank_done, groups_of(v, g))
                        dve.tensor_copy(count_g[:, :], rank_g[i][:, P - 1:GB * P:P]).then_inc(count_done, 1)
                        for k in range(GB):
                            last = dve.bn_aggr(mv_g[i][:, k, :], stats_g[:, k, :])
                        last.then_inc(mean_done, 1)
                    if c % GB == 3 and live(c + 1) and first:
                        g = (c + 1) // GB
                        dve.tensor_reduce(degree_g[g % 2][:, :], adj_g[g % 2][:, :, :], AX.X, ALU.add)\
                           .then_inc(degree_done, 1)
                    if live(c + 1):
                        b = c + 1
                        g, k = b // GB, b % GB
                        dve.wait_ge(table_done, v + b + 1)
                        dve.scalar_tensor_tensor(proj_lo[b % 2][:, :], proj_ps, rstd_g[g % 2][:, k:k + 1],
                                                 proj_hi[b % 2][:, :].bitcast(F32), ALU.mult, ALU.subtract)\
                           .then_inc(lo_done, 1)
                        dve.tensor_tensor(table[b % 2][:, 2 * P:3 * P], adjT_ps,
                                          table[b % 2][:, 0:P].bitcast(F32), ALU.subtract)\
                           .then_inc(adj_lo_done, 1)
                    if live(c + 2):
                        b = c + 2
                        g, k = b // GB, b % GB
                        dve.wait_ge(mean_done, groups_of(v, g))
                        reach(dve, xT_done, v + b)
                        dve.tensor_scalar(r[:, :], x_g[g % 2][:, k, :], mv_g[g % 2][:, k, 0:1], 0.0,
                                          ALU.subtract, ALU.max).then_inc(r_done, 1)
                    if live(c):
                        b = c
                        dve.wait_ge(rows_done, v + b + 1)
                        dve.tensor_tensor(own[:, :].rearrange("p (k n) -> p k n", k=CHUNKS),
                                          bankW[:, :, P:2 * P],
                                          number_col[:, :].unsqueeze(2).to_broadcast([P, CHUNKS, P]),
                                          ALU.is_equal).then_inc(own_done, 1)
                return step

            def flag():
                dve.wait_ge(flag_step, GROUPS)
                dve.tensor_reduce(most_1[:, :], most[:, :], AX.X, ALU.max).then_inc(flag_step, 1)
                dve.wait_ge(flag_step, GROUPS + 1)
                dve.tensor_copy(most_i[:, :], most_1[:, :]).then_inc(flag_set, 1)

            sweep(dve, vector_steps(True), 0)
            flag()
            dve.wait_ge(flag_set, 1)
            edges = dve.value_load(most_i[P - 1:P, 0:1], min_val=0, max_val=NODES * NODES)
            with dve.If(edges > EDGES):
                with dve.Fori(BATCHES, BATCHES * WINDOWS, BATCHES) as done:
                    dve.wait_ge(bound_done, groups_of(done, -1))
                    dve.tensor_scalar(window[:, :], window[:, :], float(EDGES), None, ALU.add)
                    sweep(dve, vector_steps(False), done)

        @block.tensor
        def _(pe):
            pe.wait_ge(const_set, 1)

            def tensor_steps(first):
                def step(m, v, c, live):
                    if live(c):
                        b = c
                        pe.wait_ge(src_done, v + b + 1)
                        pe.wait_ge(numbers_done, v + b + 1)
                        reach(pe, hidden_done, v + b)
                        for a in range(2):
                            last = pe.matmul(bankA[:, a, 0:HALF], numbers[b % 2][:, :],
                                             src_hot[b % 2][:, a * HALF:(a + 1) * HALF], start=True, stop=True)
                        last.then_inc(found_done, 1)
                    if live(c + 1):
                        b = c + 1
                        pe.wait_ge(r_done, v + b + 1)
                        reach(pe, lo_done, v + b)
                        reach(pe, adj_lo_done, v + b)
                        reach(pe, scaled_done, v + b - 3)
                        if b % GB == 0:
                            pe.wait_ge(bound_done, groups_of(v, b // GB))
                        pe.transpose(xT_ps, r[:, :], ident[:, :]).then_inc(xT_done, 1)
                    if live(c - 1):
                        b = c - 1
                        pe.wait_ge(hidden_done, v + b + 1)
                        reach(pe, z_sb_done, v + b)
                        for a in range(2):
                            pe.matmul(bankZ[:, a, 0:HALF].rearrange("p (k n) -> p k n", n=P), ones[:, :],
                                      b2_k[:, :].unsqueeze(1).to_broadcast([P, HALF // P, P]),
                                      start=True, stop=False, skip_group_check=True)
                            for k in range(3 * a, 3 * a + 3):
                                last = pe.matmul(z_chunk(k), chunk(hidden, k), w2_c[:, :],
                                                 start=False, stop=True, skip_group_check=True)
                        last.then_inc(z_done, 1)
                    if live(c + 1):
                        b = c + 1
                        g, k = b // GB, b % GB
                        pe.wait_ge(rT_done, v + b + 1)
                        pe.matmul(proj_ps, rT[:, :], w1_sb[:, :], start=True, stop=True)
                        pe.wait_ge(numbers_done, v + b + 1)
                        pe.wait_ge(adj_in[g % 2], loads_of(v, g))
                        pe.transpose(adjT_ps, adj_g[g % 2][:, k, :], ident[:, :])
                        pe.transpose(numT_ps, numbers[b % 2][:, :].bitcast(F32), ident[:, :])\
                          .then_inc(tableT_done, 1)
                    if live(c):
                        b = c
                        pe.wait_ge(dst_done, v + b + 1)
                        pe.wait_ge(lo_done, v + b + 1)
                        for n, (t, at, hot) in enumerate(
                                ((proj_hi, 0, src_hot[b % 2]), (proj_lo, 0, src_hot[b % 2]),
                                 (proj_hi, P, dst_hot), (proj_lo, P, dst_hot))):
                            for a in range(2):
                                last = pe.matmul(bankA[:, a, 0:HALF], t[b % 2][:, at:at + P],
                                                 hot[:, a * HALF:(a + 1) * HALF], start=(n == 0), stop=(n == 3))
                        last.then_inc(pre_done, 1)
                    if live(c):
                        b = c
                        pe.wait_ge(adj_lo_done, v + b + 1)
                        reach(pe, weight_done, v + b)
                        for k in range(CHUNKS):
                            for n in range(2):
                                last = pe.matmul(bankW[:, k, :], chunk(dst_hot, k),
                                                 table[b % 2][:, 2 * n * P:2 * (n + 1) * P],
                                                 start=(n == 0), stop=(n == 1))
                        last.then_inc(rows_done, 1)
                    if c % GB == 2 and live(c + 2):
                        g = (c + 2) // GB
                        pe.wait_ge(count_done, groups_of(v, g))
                        reach(pe, adj_lo_done, v + max(c + 2, 0))
                        reach(pe, scaled_done, v + max(c - 2, 0))
                        pe.matmul(bound_ps[:, 0:GB], before[:, :], count_g[:, :], start=True, stop=True)
                        pe.matmul(bound_ps[:, GB:2 * GB], upto[:, :], count_g[:, :], start=True, stop=True)\
                          .then_inc(boundmm_done, 1)
                    if live(c - 2):
                        b = c - 2
                        reach(pe, adj_lo_done, v + min(b + 4, BATCHES))
                        reach(pe, scaled_done, v + b)
                        pe.wait_ge(weight_done, v + b + 1)
                        pe.wait_ge(z_sb_done, v + b + 1)
                        for k in range(CHUNKS):
                            last = pe.matmul(out_ps, chunk(weight[b % 4], k), chunk(z_sb[b % 2], k),
                                             start=(k == 0), stop=(k == CHUNKS - 1))
                        last.then_inc(sum_done, 1)
                return step
            sweeps(pe, tensor_steps)


_INS = ['x', 'adj', 'L0_gnn_W1', 'L0_gnn_b1', 'L0_gnn_W2', 'L0_gnn_b2', 'L0_gnn_gamma', 'L0_gnn_beta']


def kernel(**inputs):
    import numpy as _np
    import concourse.bacc as _bacc
    from concourse import mybir as _mybir
    from concourse.bass_utils import run_bass_kernel_spmd as _run

    nc = _bacc.Bacc("TRN2", target_bir_lowering=False, num_devices=1)
    arrays, args = {}, []
    for name in _INS:
        a = _np.ascontiguousarray(inputs[name])
        arrays[f"in_{name}"] = a
        args.append(nc.dram_tensor(f"in_{name}", a.shape, _mybir.dt.from_np(a.dtype), kind="ExternalInput").ap())
    out = nc.dram_tensor("out", inputs["x"].shape, _mybir.dt.float32, kind="ExternalOutput").ap()
    gnn_layer(nc, *args, out)
    r = _run(nc, [arrays], core_ids=[0])
    return r.results[0]["out"]
```

```python
import concourse.bass as bass
from concourse import mybir
from contextlib import ExitStack


def gnn_layer(nc, x, adj, w1, b1, w2, b2, gamma, beta, out):
    F32, F32R, F16, BF16, I32 = (mybir.dt.float32, mybir.dt.float32r, mybir.dt.float16,
                                 mybir.dt.bfloat16, mybir.dt.int32)
    ALU, ACT, AX = mybir.AluOpType, mybir.ActivationFunctionType, mybir.AxisListType

    BATCHES, NODES, FEAT = x.shape
    P = 128
    CHUNKS = 6
    EDGES = CHUNKS * P
    HALF = EDGES // 2
    WINDOWS = -(-NODES * NODES // EDGES)
    GB = 4
    GROUPS = BATCHES // GB
    BODY = 2 * GB
    HEAD = 2 * GB
    LOOPED = BATCHES - HEAD - BODY
    EPS = 1e-05
    PARAMS = 7
    WARM = 7
    assert NODES == P and FEAT == P and LOOPED % BODY == 0

    x_d = x.rearrange("b n f -> n b f")
    adj_d = adj.rearrange("b n m -> n b m")
    out_d = out.rearrange("b n f -> n b f")

    ctx = ExitStack()
    with ctx:
        def sb(name, shape, dt=F32):
            return ctx.enter_context(nc.sbuf_tensor(name, shape, dt))

        def pb(name, shape, dt=F32):
            return ctx.enter_context(nc.psum_tensor(name, shape, dt))

        def sem(name):
            return ctx.enter_context(nc.semaphore(name))

        ident = sb("ident", [P, P])
        before = sb("before", [P, P], BF16)
        upto = sb("upto", [P, P], BF16)
        minus_half = sb("minus_half", [P, CHUNKS])
        eps_x = sb("eps_x", [P, GB])
        eps_z = sb("eps_z", [P, CHUNKS])
        tri = sb("tri", [P, P])
        ones = sb("ones", [P, P], BF16)
        ones_f = sb("ones_f", [P, P])
        position = sb("position", [P, EDGES], F16)
        number = sb("number", [P, EDGES], F16)
        number_col = sb("number_col", [P, CHUNKS])
        restart = sb("restart", [P, GB * P], BF16)
        w1_sb = sb("w1_sb", [P, 2 * P])
        b1_col = sb("b1_col", [P, 1])
        w2_in = sb("w2_in", [P, P])
        w2_c = sb("w2_c", [P, P])
        b2_all = sb("b2_all", [P, P])
        b2_c = sb("b2_c", [P, P])
        mean_w = sb("mean_w", [P, 2])
        gamma_all = sb("gamma_all", [P, P])
        gamma_s = sb("gamma_s", [P, P])
        beta_all = sb("beta_all", [P, P])
        window = sb("window", [P, 1])
        most = sb("most", [P, GB])
        most_1 = sb("most_1", [P, 1])
        most_i = sb("most_i", [P, 1], I32)

        x_g = [sb(f"x_g{i}", [P, GB, P]) for i in range(2)]
        adj_g = [sb(f"adj_g{i}", [P, GB, P]) for i in range(2)]
        res_g = [sb(f"res_g{i}", [P, GB, P]) for i in range(2)]
        out_g = [sb(f"out_g{i}", [P, GB, P]) for i in range(2)]
        edge_g = [sb(f"edge_g{i}", [P, GB * P], BF16) for i in range(2)]
        rank_g = [sb(f"rank_g{i}", [P, GB * P]) for i in range(2)]
        count_g = sb("count_g", [P, GB], BF16)
        bound_g = [sb(f"bound_g{i}", [P, 2 * GB]) for i in range(2)]
        stats_g = sb("stats_g", [P, GB, 6])
        mv_g = [sb(f"mv_g{i}", [P, GB, 2]) for i in range(2)]
        rstd_g = [sb(f"rstd_g{i}", [P, GB]) for i in range(2)]
        degree_g = [sb(f"degree_g{i}", [P, GB]) for i in range(2)]

        r = sb("r", [P, P])
        rT = sb("rT", [P, P])
        numbers = [sb(f"numbers{i}", [P, P], F32R) for i in range(2)]
        past = sb("past", [P, EDGES], F16)
        src_hot = [sb(f"src_hot{i}", [P, EDGES], F32R) for i in range(2)]
        dst_hot = sb("dst_hot", [P, EDGES], F32R)
        proj_hi = [sb(f"proj_hi{i}", [P, 2 * P], F32R) for i in range(2)]
        proj_lo = [sb(f"proj_lo{i}", [P, 2 * P], F32R) for i in range(2)]
        table = [sb(f"table{i}", [P, 4 * P], F32R) for i in range(2)]
        hidden = sb("hidden", [P, EDGES])
        z_sb = [sb(f"z_sb{i}", [P, EDGES]) for i in range(2)]
        square = sb("square", [P, EDGES])
        sumsq = sb("sumsq", [P, CHUNKS])
        rstd = sb("rstd", [P, CHUNKS])
        own = sb("own", [P, EDGES], BF16)
        weight = [sb(f"weight{i}", [P, EDGES]) for i in range(4)]
        scaled = [sb(f"scaled{i}", [P, P]) for i in range(2)]
        xvar = sb("xvar", [P, GB])
        var = sb("var", [P, CHUNKS])
        scratch = sb("scratch", [P, GB])
        beta_x = sb("beta_x", [P, P])

        bankA = pb("bankA", [P, 2, 512])
        bankZ = pb("bankZ", [P, 2, 512])
        bankW = pb("bankW", [P, CHUNKS, 2 * P])
        bankH = pb("bankH", [P, 512])
        edges_ps = bankA[:, :, 0:HALF]
        out_ps = bankH[:, 0:P]
        bound_ps = bankH[:, 2 * P:2 * P + 2 * GB]
        xT_ps = bankH[:, 0:P]
        proj_ps = bankH[:, 0:2 * P]
        adjT_ps = bankH[:, 2 * P:3 * P]
        numT_ps = bankH[:, 3 * P:4 * P]

        def halves(t):
            return t.rearrange("p (a n) -> p a n", a=2)

        def chunk(t, k):
            return t[:, k * P:(k + 1) * P]

        def z_chunk(k):
            return bankZ[:, k // 3, (k % 3) * P:(k % 3 + 1) * P]

        r_done = sem("r_done")
        xT_done = sem("xT_done")
        rT_done = sem("rT_done")
        lo_done = sem("lo_done")
        numbers_done = sem("numbers_done")
        past_done = sem("past_done")
        src_done = sem("src_done")
        proj_done = sem("proj_done")
        table_done = sem("table_done")
        adj_lo_done = sem("adj_lo_done")
        found_done = sem("found_done")
        dst_done = sem("dst_done")
        pre_done = sem("pre_done")
        hidden_done = sem("hidden_done")
        z_done = [sem(f"z_done{a}") for a in range(2)]
        bias_done = [sem(f"bias_done{a}") for a in range(2)]
        sumsq_done = sem("sumsq_done")
        z_sb_done = [sem(f"z_sb_done{a}") for a in range(2)]
        var_done = sem("var_done")
        rstd_done = sem("rstd_done")
        rows_done = sem("rows_done")
        own_done = sem("own_done")
        weight_done = sem("weight_done")
        sum_done = sem("sum_done")
        scaled_done = sem("scaled_done")
        beta_done = sem("beta_done")
        base_done = sem("base_done")
        out_done = sem("out_done")
        edge_done = sem("edge_done")
        rank_done = sem("rank_done")
        count_done = sem("count_done")
        boundmm_done = sem("boundmm_done")
        bound_done = sem("bound_done")
        stats_done = sem("stats_done")
        mean_done = sem("mean_done")
        xvar_done = sem("xvar_done")
        xrstd_done = sem("xrstd_done")
        degree_done = sem("degree_done")
        x_in = [sem(f"x_in{i}") for i in range(2)]
        adj_in = [sem(f"adj_in{i}") for i in range(2)]
        res_in = [sem(f"res_in{i}") for i in range(2)]
        stored = [sem(f"stored{i}") for i in range(2)]
        params_in = sem("params_in")
        pool_set = sem("pool_set")
        const_set = sem("const_set")
        marked = sem("marked")
        window_set = sem("window_set")
        flag_step = sem("flag_step")
        flag_set = sem("flag_set")

        block = ctx.enter_context(nc.Block())

        def reach(eng, s, value):
            if not isinstance(value, int) or value > 0:
                eng.wait_ge(s, value)

        def sweep(eng, step, done):
            for c in range(-3, HEAD):
                step(0, done, c, lambda b: 0 <= b < BATCHES)
            with eng.Fori(0, LOOPED - BODY + 1, BODY) as m:
                for c in range(HEAD, HEAD + BODY):
                    step(m, m + done, c, lambda b: True)
            for c in range(HEAD + LOOPED, BATCHES + GB):
                step(0, done, c, lambda b: 0 <= b < BATCHES)

        def sweeps(eng, make):
            sweep(eng, make(True), 0)
            eng.wait_ge(flag_set, 1)
            edges = eng.value_load(most_i[P - 1:P, 0:1], min_val=0, max_val=NODES * NODES)
            with eng.If(edges > EDGES):
                with eng.Fori(BATCHES, BATCHES * WINDOWS, BATCHES) as done:
                    sweep(eng, make(False), done)

        def groups_of(v, g):
            return (v // GB if isinstance(v, int) else v * 1 // GB) + g + 1

        def loads_of(v, g):
            return v * (16 // (2 * GB)) + 16 * (g // 2 + 1)

        @block.sync
        def _(sp):
            sp.dma_start(x_g[0][:, :, :], x_d[:, 0:GB, :]).then_inc(x_in[0], 16)
            sp.dma_start(adj_g[0][:, :, :], adj_d[:, 0:GB, :]).then_inc(adj_in[0], 16)
            for dst, src in ((w1_sb[:, 0:P], w1[0:P, :]), (w1_sb[:, P:2 * P], w1[P:2 * P, :]),
                             (b1_col[:, :], b1.rearrange("(k a) -> k a", a=1)), (w2_in[:, :], w2),
                             (b2_all[:, :], b2.partition_broadcast(P)),
                             (gamma_all[:, :], gamma.partition_broadcast(P)),
                             (beta_all[:, :], beta.partition_broadcast(P))):
                sp.dma_start(dst, src).then_inc(params_in, 16)

            def held(value):
                return value if isinstance(value, int) else sp.snap(value)

            def sync_steps(first):
                def step(m, v, c, live):
                    if c % GB == 3 and live(c - 4):
                        g = (c - 4) // GB
                        at = bass.ds(held(m + GB * g), GB)
                        sp.wait_ge(out_done, v + c - 4 + 1)
                        sp.dma_start(out_d[:, at, :], out_g[g % 2][:, :, :]).then_inc(stored[g % 2], 16)
                    g = c // GB + 1
                    if (c % GB == 0 or c == -3 and not first) and live(GB * g):
                        i = g % 2
                        at = bass.ds(held(m + GB * g), GB)
                        used = held(v + GB * (g - 1))
                        if not first:
                            used_out = held(v + GB * (g - 2) + GB)
                            last_store = held(loads_of(v, g) - 16 * GROUPS // 2)
                        if first:
                            reach(sp, base_done, used)
                        reach(sp, r_done, used)
                        reach(sp, proj_done, used)
                        sp.dma_start(x_g[i][:, :, :], x_d[:, at, :]).then_inc(x_in[i], 16)
                        sp.dma_start(adj_g[i][:, :, :], adj_d[:, at, :]).then_inc(adj_in[i], 16)
                        if not first:
                            sp.wait_ge(stored[i], last_store)
                            sp.wait_ge(out_done, used_out)
                            sp.dma_start(res_g[i][:, :, :], out_d[:, at, :]).then_inc(res_in[i], 16)
                return step

            def all_stored(windows):
                for i in range(2):
                    sp.wait_ge(stored[i], 16 * (GROUPS // 2) * windows)

            sweep(sp, sync_steps(True), 0)
            all_stored(1)
            sp.wait_ge(flag_set, 1)
            edges = sp.value_load(most_i[P - 1:P, 0:1], min_val=0, max_val=NODES * NODES)
            with sp.If(edges > EDGES):
                with sp.Fori(BATCHES, BATCHES * WINDOWS, BATCHES) as done:
                    sweep(sp, sync_steps(False), done)
                all_stored(WINDOWS)

        @block.gpsimd
        def _(pool):
            pool.iota(position[:, :], [[1, EDGES]], base=0, channel_multiplier=0,
                      allow_small_or_imprecise_dtypes=True).then_inc(pool_set, 1)
            pool.iota(number_col[:, :], [[P, CHUNKS]], base=1, channel_multiplier=1,
                      allow_small_or_imprecise_dtypes=True).then_inc(pool_set, 1)
            pool.memset(ones_f[:, :], 1.0).then_inc(pool_set, 1)
            pool.memset(minus_half[:, :], -0.5).then_inc(pool_set, 1)
            pool.memset(eps_x[:, :], EPS).then_inc(pool_set, 1)
            pool.memset(eps_z[:, :], EPS * FEAT).then_inc(pool_set, 1)
            pool.wait_ge(pool_set, 6)
            for dst, op, base in ((ident, ALU.is_equal, 0), (tri, ALU.is_gt, 0)):
                pool.affine_select(out=dst[:, :], in_=ones_f[:, :], compare_op=op, fill=0.0, base=base,
                                   pattern=[[1, P]], channel_multiplier=-1).then_inc(pool_set, 1)

            def pool_steps(first):
                def step(m, v, c, live):
                    b = c
                    if live(b) and first:
                        g, k = b // GB, b % GB
                        if b == 0:
                            pool.wait_ge(params_in, 16 * PARAMS)
                        pool.wait_ge(degree_done, (m // GB) + g + 1)
                        pool.wait_ge(x_in[g % 2], loads_of(v, g))
                        reach(pool, stored[g % 2], loads_of(v, g - 2))
                        reach(pool, base_done, v + b)
                        pool.tensor_tensor(beta_x[:, :], beta_all[:, :],
                                           degree_g[g % 2][:, k:k + 1].to_broadcast([P, P]),
                                           ALU.mult).then_inc(beta_done, 1)
                        pool.wait_ge(beta_done, v + b + 1)
                        pool.tensor_tensor(out_g[g % 2][:, k, :], x_g[g % 2][:, k, :], beta_x[:, :],
                                           ALU.add).then_inc(base_done, 1)
                    if live(c - 1):
                        b = c - 1
                        pool.wait_ge(sumsq_done, v + b + 1)
                        reach(pool, z_sb_done[1], v + b)
                        pool.tensor_tensor(var[:, :], sumsq[:, :], eps_z[:, :],
                                           ALU.add).then_inc(var_done, 1)
                        pool.wait_ge(var_done, v + b + 1)
                        pool.tensor_tensor(rstd[:, :], var[:, :], minus_half[:, :],
                                           ALU.pow).then_inc(rstd_done, 1)
                    b = c - 3
                    if live(b):
                        g, k = b // GB, b % GB
                        if first:
                            base = out_g[g % 2]
                            pool.wait_ge(base_done, v + b + 1)
                        else:
                            base = res_g[g % 2]
                            pool.wait_ge(res_in[g % 2], loads_of(v, g) - 16 * GROUPS // 2)
                            pool.wait_ge(stored[g % 2], loads_of(v, g - 2))
                        pool.wait_ge(scaled_done, v + b + 1)
                        pool.tensor_tensor(out_g[g % 2][:, k, :], base[:, k, :], scaled[b % 2][:, :],
                                           ALU.add).then_inc(out_done, 1)
                    if c % GB == 2 and live(c + 2):
                        g = (c + 2) // GB
                        pool.wait_ge(mean_done, groups_of(v, g))
                        reach(pool, xrstd_done, groups_of(v, g - 1))
                        pool.tensor_tensor(xvar[:, :], mv_g[g % 2][:, :, 1], eps_x[:, :],
                                           ALU.add).then_inc(xvar_done, 1)
                        pool.wait_ge(xvar_done, groups_of(v, g))
                        pool.tensor_tensor(rstd_g[g % 2][:, :], xvar[:, :], minus_half[:, 0:GB],
                                           ALU.pow).then_inc(xrstd_done, 1)
                return step
            sweeps(pool, pool_steps)

        @block.scalar
        def _(act):
            act.wait_ge(pool_set, 6)
            act.activation(scratch[:, :], eps_x[:, :], ACT.Copy)

            def scalar_steps(first):
                def step(m, v, c, live):
                    if live(c + 1):
                        b = c + 1
                        act.wait_ge(xT_done, v + b + 1)
                        act.activation(rT[:, :], xT_ps, ACT.Copy).then_inc(rT_done, 1)
                    if live(c - 1):
                        b = c - 1
                        reach(act, rstd_done, v + b)
                        for a in range(2):
                            act.wait_ge(z_done[a], v + b + 1)
                            for k in range(3 * a, 3 * a + 3):
                                last = act.activation(chunk(square, k), z_chunk(k), ACT.Square,
                                                      accum_out=sumsq[:, k:k + 1])
                        last.then_inc(sumsq_done, 1)
                    if live(c + 1):
                        b = c + 1
                        g, k = b // GB, b % GB
                        act.wait_ge(proj_done, v + b + 1)
                        act.wait_ge(xrstd_done, groups_of(v, g))
                        act.activation(proj_hi[b % 2][:, :], proj_ps, ACT.Copy,
                                       scale=rstd_g[g % 2][:, k:k + 1])
                        act.activation(table[b % 2][:, 0:2 * P], bankH[:, 2 * P:4 * P], ACT.Copy)\
                           .then_inc(table_done, 1)
                    if live(c):
                        b = c
                        if first and c == 0:
                            act.wait_ge(params_in, 16 * PARAMS)
                        act.wait_ge(pre_done, v + b + 1)
                        act.activation(halves(hidden[:, :]), edges_ps, ACT.Relu, bias=b1_col[:, 0:1])\
                           .then_inc(hidden_done, 1)
                    for a, chunks in ((0, (0, 1, 2, 3)), (1, (4, 5))):
                        if live(c - 1):
                            b = c - 1
                            if a == 0:
                                act.wait_ge(rstd_done, v + b + 1)
                                reach(act, sum_done, v + b - 1)
                            for k in chunks:
                                ins = act.activation(chunk(z_sb[b % 2], k), z_chunk(k), ACT.Copy,
                                                     scale=rstd[:, k:k + 1])
                                if k % 3 == 2:
                                    ins.then_inc(z_sb_done[a], 1)
                        if live(c):
                            if first and c == 0 and a == 0:
                                act.wait_ge(marked, 1)
                                act.wait_ge(const_set, 2)
                            reach(act, z_sb_done[a], v + c)
                            act.activation(bankZ[:, a, 0:HALF].rearrange("p (k n) -> p k n", n=P),
                                           b2_c[:, :].unsqueeze(1).to_broadcast([P, HALF // P, P]),
                                           ACT.Copy).then_inc(bias_done[a], 1)
                return step
            sweeps(act, scalar_steps)

        @block.vector
        def _(dve):
            made = [0]

            def then(ins):
                made[0] += 1
                ins.then_inc(window_set, 1)
                dve.wait_ge(window_set, made[0])

            dve.memset(ones[:, :], 1.0)
            then(dve.memset(restart[:, :], 1.0))
            dve.memset(window[:, :], 0.0)
            dve.memset(most[:, :], 0.0)
            for t in table:
                dve.memset(t[:, 3 * P:4 * P].bitcast(F32), 0.0)
            then(dve.memset(restart[:, :].rearrange("p (b n) -> p b n", b=GB)[:, :, 0:1], 0.0))
            dve.wait_ge(pool_set, 8)
            dve.tensor_scalar(number[:, :], position[:, :], 1.0, None, ALU.add)
            dve.tensor_copy(before[:, :], tri[:, :])
            dve.tensor_tensor(upto[:, :], tri[:, :], ident[:, :], ALU.add).then_inc(const_set, 1)

            def parameters():
                dve.wait_ge(params_in, 16 * PARAMS)
                dve.tensor_reduce(mean_w[:, 0:1], w2_in[:, :], AX.X, ALU.add)
                then(dve.tensor_reduce(mean_w[:, 1:2], b2_all[:, :], AX.X, ALU.add))
                then(dve.tensor_scalar(mean_w[:, :], mean_w[:, :], 1.0 / FEAT, None, ALU.mult))
                dve.tensor_scalar(w2_c[:, :], w2_in[:, :], mean_w[:, 0:1], None, ALU.subtract)
                dve.tensor_scalar(b2_c[:, :], b2_all[:, :], mean_w[:, 1:2], None, ALU.subtract)
                dve.tensor_scalar(gamma_s[:, :], gamma_all[:, :], float(FEAT) ** 0.5, None, ALU.mult)\
                   .then_inc(const_set, 1)

            def number_edges(v, b):
                g, k = b // GB, b % GB
                at = slice(k * P, (k + 1) * P)
                first_edge = bound_g[g % 2][:, k:k + 1]
                end_edge = bound_g[g % 2][:, GB + k:GB + k + 1]
                dve.wait_ge(bound_done, groups_of(v, g))
                dve.scalar_tensor_tensor(numbers[b % 2][:, :], rank_g[g % 2][:, at], first_edge,
                                         edge_g[g % 2][:, at], ALU.add, ALU.mult)\
                   .then_inc(numbers_done, 1)
                reach(dve, src_done, v + b)
                dve.tensor_scalar(past[:, :], position[:, :], end_edge, None, ALU.is_ge)\
                   .then_inc(past_done, 1)

            def vector_steps(first):
                def step(m, v, c, live):
                    if c % GB != 3 and live(c + 1):
                        number_edges(v, c + 1)
                    if c % GB == 3 and live(c + 1):
                        g = (c + 1) // GB
                        dve.wait_ge(boundmm_done, groups_of(v, g))
                        dve.tensor_scalar(bound_g[g % 2][:, :], bound_ps, window[:, 0:1], None, ALU.subtract)\
                           .then_inc(bound_done, 1)
                    if live(c - 3):
                        b = c - 3
                        dve.wait_ge(sum_done, v + b + 1)
                        reach(dve, out_done, v + b - 1)
                        dve.tensor_tensor(scaled[b % 2][:, :], out_ps, gamma_s[:, :],
                                          ALU.mult).then_inc(scaled_done, 1)
                    if c % GB == 3 and live(c + 1):
                        number_edges(v, c + 1)
                    if live(c):
                        b = c
                        dve.wait_ge(found_done, v + b + 1)
                        dve.tensor_tensor(halves(dst_hot[:, :]), edges_ps, halves(number[:, :]),
                                          ALU.is_equal).then_inc(dst_done, 1)
                    if live(c - 1):
                        b = c - 1
                        dve.wait_ge(own_done, v + b + 1)
                        reach(dve, sum_done, v + b - 3)
                        dve.tensor_tensor(weight[b % 4][:, :].rearrange("p (k n) -> p k n", k=CHUNKS),
                                          bankW[:, :, 0:P],
                                          own[:, :].rearrange("p (k n) -> p k n", k=CHUNKS),
                                          ALU.mult).then_inc(weight_done, 1)
                    if live(c + 1):
                        b = c + 1
                        g, k = b // GB, b % GB
                        first_edge = bound_g[g % 2][:, k:k + 1]
                        dve.wait_ge(past_done, v + b + 1)
                        dve.scalar_tensor_tensor(src_hot[b % 2][:, :], position[:, :], first_edge,
                                                 past[:, :], ALU.is_ge, ALU.subtract)\
                           .then_inc(src_done, 1)
                    if c % GB == 1 and live(c + 3):
                        g = (c + 3) // GB
                        i = g % 2
                        dve.wait_ge(adj_in[i], loads_of(v, g))
                        dve.tensor_scalar(edge_g[i][:, :], adj_g[i][:, :, :].rearrange("p b n -> p (b n)"),
                                          0.0, None, ALU.not_equal).then_inc(edge_done, 1)
                        dve.wait_ge(x_in[i], loads_of(v, g))
                        dve.bn_stats(stats_g[:, 0, :], x_g[i][:, 0, :])
                    if c % GB == 2 and live(c + 2):
                        g = (c + 2) // GB
                        i = g % 2
                        for k in range(1, GB):
                            last = dve.bn_stats(stats_g[:, k, :], x_g[i][:, k, :])
                        last.then_inc(stats_done, 1)
                    if first and c == 0:
                        parameters()
                    if live(c + 1):
                        b = c + 1
                        g, k = b // GB, b % GB
                        dve.wait_ge(table_done, v + b + 1)
                        dve.scalar_tensor_tensor(proj_lo[b % 2][:, :], proj_ps, rstd_g[g % 2][:, k:k + 1],
                                                 proj_hi[b % 2][:, :].bitcast(F32), ALU.mult, ALU.subtract)\
                           .then_inc(lo_done, 1)
                        dve.tensor_tensor(table[b % 2][:, 2 * P:3 * P], adjT_ps,
                                          table[b % 2][:, 0:P].bitcast(F32), ALU.subtract)\
                           .then_inc(adj_lo_done, 1)
                    if c % GB == 2 and live(c + 2):
                        g = (c + 2) // GB
                        i = g % 2
                        dve.wait_ge(stats_done, groups_of(v, g))
                        dve.wait_ge(rank_done, groups_of(v, g))
                        dve.tensor_copy(count_g[:, :], rank_g[i][:, P - 1:GB * P:P]).then_inc(count_done, 1)
                        for k in range(GB):
                            last = dve.bn_aggr(mv_g[i][:, k, :], stats_g[:, k, :])
                        last.then_inc(mean_done, 1)
                    if live(c + 2):
                        b = c + 2
                        g, k = b // GB, b % GB
                        dve.wait_ge(mean_done, groups_of(v, g))
                        reach(dve, xT_done, v + b)
                        dve.tensor_scalar(r[:, :], x_g[g % 2][:, k, :], mv_g[g % 2][:, k, 0:1], 0.0,
                                          ALU.subtract, ALU.max).then_inc(r_done, 1)
                    if c % GB == 1 and live(c + 3):
                        g = (c + 3) // GB
                        i = g % 2
                        dve.wait_ge(edge_done, groups_of(v, g))
                        dve.tensor_tensor_scan(rank_g[i][:, :], restart[:, :], edge_g[i][:, :], 0.0,
                                               ALU.mult, ALU.add).then_inc(rank_done, 1)
                    if c % GB == 3 and live(c + 1) and first:
                        g = (c + 1) // GB
                        dve.tensor_tensor(most[:, :], bound_g[g % 2][:, GB:2 * GB], most[:, :], ALU.max)\
                           .then_inc(flag_step, 1)
                    if (c % GB == 3 and c > 0 and live(c + 1) or c == 0) and first:
                        g = (c + 1) // GB
                        dve.tensor_reduce(degree_g[g % 2][:, :], adj_g[g % 2][:, :, :], AX.X, ALU.add)\
                           .then_inc(degree_done, 1)
                    if live(c):
                        b = c
                        dve.wait_ge(rows_done, v + b + 1)
                        dve.tensor_tensor(own[:, :].rearrange("p (k n) -> p k n", k=CHUNKS),
                                          bankW[:, :, P:2 * P],
                                          number_col[:, :].unsqueeze(2).to_broadcast([P, CHUNKS, P]),
                                          ALU.is_equal).then_inc(own_done, 1)
                return step

            def flag():
                dve.wait_ge(flag_step, GROUPS)
                dve.tensor_reduce(most_1[:, :], most[:, :], AX.X, ALU.max).then_inc(flag_step, 1)
                dve.wait_ge(flag_step, GROUPS + 1)
                dve.tensor_copy(most_i[:, :], most_1[:, :]).then_inc(flag_set, 1)

            sweep(dve, vector_steps(True), 0)
            flag()
            dve.wait_ge(flag_set, 1)
            edges = dve.value_load(most_i[P - 1:P, 0:1], min_val=0, max_val=NODES * NODES)
            with dve.If(edges > EDGES):
                with dve.Fori(BATCHES, BATCHES * WINDOWS, BATCHES) as done:
                    dve.wait_ge(bound_done, groups_of(done, -1))
                    dve.tensor_scalar(window[:, :], window[:, :], float(EDGES), None, ALU.add)
                    sweep(dve, vector_steps(False), done)

        @block.tensor
        def _(pe):
            def fill(count):
                for n in range(count):
                    ins = pe.matmul(bankZ[:, n % 2, 0:HALF].rearrange("p (k n) -> p k n", n=P), ones[:, :],
                                    ones[:, :].unsqueeze(1).to_broadcast([P, HALF // P, P]),
                                    start=True, stop=True, skip_group_check=True)
                return ins

            pe.wait_ge(window_set, 1)
            fill(2 * WARM)
            pe.wait_ge(const_set, 1)

            def tensor_steps(first):
                def step(m, v, c, live):
                    if live(c):
                        b = c
                        pe.wait_ge(src_done, v + b + 1)
                        pe.wait_ge(numbers_done, v + b + 1)
                        reach(pe, hidden_done, v + b)
                        for a in range(2):
                            last = pe.matmul(bankA[:, a, 0:HALF], numbers[b % 2][:, :],
                                             src_hot[b % 2][:, a * HALF:(a + 1) * HALF], start=True, stop=True)
                        last.then_inc(found_done, 1)
                    if first and c == 0:
                        fill(2 * WARM).then_inc(marked, 1)
                    for a in range(2):
                        if live(c - 1):
                            b = c - 1
                            pe.wait_ge(hidden_done, v + b + 1)
                            pe.wait_ge(bias_done[a], v + b + 1)
                            for k in range(3 * a, 3 * a + 3):
                                last = pe.matmul(z_chunk(k), chunk(hidden, k), w2_c[:, :],
                                                 start=False, stop=True, skip_group_check=True)
                            last.then_inc(z_done[a], 1)
                        if live(c + 1) and a == 0:
                            b = c + 1
                            g, k = b // GB, b % GB
                            pe.wait_ge(r_done, v + b + 1)
                            reach(pe, adj_lo_done, v + b)
                            reach(pe, scaled_done, v + b - 3)
                            if b % GB == 0:
                                pe.wait_ge(bound_done, groups_of(v, b // GB))
                            pe.wait_ge(numbers_done, v + b + 1)
                            pe.wait_ge(adj_in[g % 2], loads_of(v, g))
                            pe.transpose(adjT_ps, adj_g[g % 2][:, k, :], ident[:, :])
                            pe.transpose(numT_ps, numbers[b % 2][:, :].bitcast(F32), ident[:, :])
                            pe.transpose(xT_ps, r[:, :], ident[:, :]).then_inc(xT_done, 1)
                    if live(c + 1):
                        b = c + 1
                        g, k = b // GB, b % GB
                        if first and b == 0:
                            pe.wait_ge(params_in, 16 * PARAMS)
                        pe.wait_ge(rT_done, v + b + 1)
                        pe.matmul(proj_ps, rT[:, :], w1_sb[:, :], start=True, stop=True).then_inc(proj_done, 1)
                    if live(c):
                        b = c
                        pe.wait_ge(dst_done, v + b + 1)
                        pe.wait_ge(lo_done, v + b + 1)
                        for n, (t, at, hot) in enumerate(
                                ((proj_hi, 0, src_hot[b % 2]), (proj_lo, 0, src_hot[b % 2]),
                                 (proj_hi, P, dst_hot), (proj_lo, P, dst_hot))):
                            for a in range(2):
                                last = pe.matmul(bankA[:, a, 0:HALF], t[b % 2][:, at:at + P],
                                                 hot[:, a * HALF:(a + 1) * HALF], start=(n == 0), stop=(n == 3))
                        last.then_inc(pre_done, 1)
                    if live(c):
                        b = c
                        pe.wait_ge(adj_lo_done, v + b + 1)
                        reach(pe, weight_done, v + b)
                        for k in range(CHUNKS):
                            for n in range(2):
                                last = pe.matmul(bankW[:, k, :], chunk(dst_hot, k),
                                                 table[b % 2][:, 2 * n * P:2 * (n + 1) * P],
                                                 start=(n == 0), stop=(n == 1))
                        last.then_inc(rows_done, 1)
                    if live(c - 2):
                        b = c - 2
                        reach(pe, adj_lo_done, v + min(b + 4, BATCHES))
                        reach(pe, scaled_done, v + b)
                        pe.wait_ge(weight_done, v + b + 1)
                        pe.wait_ge(z_sb_done[1], v + b + 1)
                        for k in range(CHUNKS):
                            last = pe.matmul(out_ps, chunk(weight[b % 4], k), chunk(z_sb[b % 2], k),
                                             start=(k == 0), stop=(k == CHUNKS - 1))
                        last.then_inc(sum_done, 1)
                    if c % GB == 2 and live(c + 2):
                        g = (c + 2) // GB
                        pe.wait_ge(count_done, groups_of(v, g))
                        reach(pe, adj_lo_done, v + max(c + 2, 0))
                        reach(pe, scaled_done, v + max(c - 2, 0))
                        pe.matmul(bound_ps[:, 0:GB], before[:, :], count_g[:, :], start=True, stop=True)
                        pe.matmul(bound_ps[:, GB:2 * GB], upto[:, :], count_g[:, :], start=True, stop=True)\
                          .then_inc(boundmm_done, 1)
                return step
            sweeps(pe, tensor_steps)


_INS = ['x', 'adj', 'L0_gnn_W1', 'L0_gnn_b1', 'L0_gnn_W2', 'L0_gnn_b2', 'L0_gnn_gamma', 'L0_gnn_beta']


def kernel(**inputs):
    import numpy as _np
    import concourse.bacc as _bacc
    from concourse import mybir as _mybir
    from concourse.bass_utils import run_bass_kernel_spmd as _run

    nc = _bacc.Bacc("TRN2", target_bir_lowering=False, num_devices=1)
    arrays, args = {}, []
    for name in _INS:
        a = _np.ascontiguousarray(inputs[name])
        arrays[f"in_{name}"] = a
        args.append(nc.dram_tensor(f"in_{name}", a.shape, _mybir.dt.from_np(a.dtype), kind="ExternalInput").ap())
    out = nc.dram_tensor("out", inputs["x"].shape, _mybir.dt.float32, kind="ExternalOutput").ap()
    gnn_layer(nc, *args, out)
    r = _run(nc, [arrays], core_ids=[0])
    return r.results[0]["out"]
```
